# Optimizing a Trainium2 kernel written in Bass

```python
import numpy as np
import jax
import jax.numpy as jnp

def _softmax(x, axis=-1):
    return jax.nn.softmax(x, axis=axis)

def _gelu(x):
    return jax.nn.gelu(x, approximate=True)

def _silu(x):
    return jax.nn.silu(x)

def _sigmoid(x):
    return jax.nn.sigmoid(x)

def _layernorm(x, axis=-1, eps=1e-05):
    m = jnp.mean(x, axis=axis, keepdims=True)
    v = jnp.var(x, axis=axis, keepdims=True)
    return (x - m) / jnp.sqrt(v + eps)

def _scatter_add(tgt, idx, src, axis=0):
    return tgt.at[idx].add(src)

def _segment_sum(src, seg, n):
    return jax.ops.segment_sum(src, seg, n)
kernel_name = 'mk_seq_preln_d2_jaxref_r4_d866c9'

def setup_inputs(seed: int=0):
    np.random.seed(seed)
    _w = jnp.asarray

    def _L0_attn_setup():
        import jax, jax.numpy as jnp
        import numpy as np
        EMBED_DIM = 256
        NUM_HEADS = 16
        HEAD_DIM = EMBED_DIM // NUM_HEADS
        EPSILON = 1e-06
        SCORE_SCALE = 1.0
        B, L = (2, 512)
        key = jax.random.key(seed)
        k0, k1, k2, k3, k4 = jax.random.split(key, 5)
        s_in = 1.0 / np.sqrt(EMBED_DIM)
        return {'x': jax.random.normal(k0, (B, L, EMBED_DIM), dtype=jnp.float32), 'w_qkv': jax.random.normal(k1, (EMBED_DIM, 3 * EMBED_DIM), dtype=jnp.float32) * s_in, 'b_qkv': jnp.zeros((3 * EMBED_DIM,), dtype=jnp.float32), 'w_out': jax.random.normal(k2, (EMBED_DIM, EMBED_DIM), dtype=jnp.float32) * s_in, 'b_out': jnp.zeros((EMBED_DIM,), dtype=jnp.float32)}
    _L0_attn_in = _L0_attn_setup()

    def _L0_ffn_setup():
        import jax, jax.numpy as jnp
        import numpy as np
        D_MODEL, D_FF, RANK = (256, 1024, 64)
        B, S = (4, 1024)
        key = jax.random.key(seed)
        ks = jax.random.split(key, 7)
        return {'x': jax.random.normal(ks[0], (B, S, D_MODEL), dtype=jnp.float32), 'U1': jax.random.normal(ks[1], (D_MODEL, RANK), dtype=jnp.float32) * 0.02, 'V1': jax.random.normal(ks[2], (RANK, D_FF), dtype=jnp.float32) * 0.02, 'b1': jnp.zeros((D_FF,), dtype=jnp.float32), 'U2': jax.random.normal(ks[3], (D_FF, RANK), dtype=jnp.float32) * 0.02, 'V2': jax.random.normal(ks[4], (RANK, D_MODEL), dtype=jnp.float32) * 0.02, 'b2': jnp.zeros((D_MODEL,), dtype=jnp.float32)}
    _L0_ffn_in = _L0_ffn_setup()

    def _L1_attn_setup():
        import jax, jax.numpy as jnp
        import numpy as np
        B, C, D, H = (2, 512, 256, 16)
        HE = D // H
        key = jax.random.key(seed)
        k1, k2, k3, k4, k5 = jax.random.split(key, 5)
        s = 0.02
        return {'x': jax.random.normal(k1, (B, C, D), dtype=jnp.float32), 'Wqkv': jax.random.normal(k2, (HE, 3 * HE), dtype=jnp.float32) * s, 'bqkv': jax.random.normal(k3, (3 * HE,), dtype=jnp.float32) * s, 'Wr': jax.random.normal(k4, (D, D), dtype=jnp.float32) * s, 'br': jax.random.normal(k5, (D,), dtype=jnp.float32) * s}
    _L1_attn_in = _L1_attn_setup()

    def _L1_ffn_setup():
        import jax, jax.numpy as jnp
        import numpy as np
        EPS = 1e-08

        def _ternary_linear(x, w):
            alpha = jnp.mean(jnp.abs(w))
            w_t = jnp.sign(w) * (jnp.abs(w) > 0.5 * alpha).astype(w.dtype)
            w_q = w + jax.lax.stop_gradient(w_t - w)
            d = x.shape[-1]
            rms = jnp.sqrt(jnp.sum(x * x, axis=-1, keepdims=True)) / jnp.sqrt(jnp.asarray(d, x.dtype))
            x_norm = x / (rms + EPS)
            return jnp.einsum('bsd,fd->bsf', x_norm, w_q)
        key = jax.random.key(seed)
        k1, k2, k3 = jax.random.split(key, 3)
        d_model, d_ff = (256, 1024)
        B, S = (4, 1024)
        x = jax.random.normal(k1, (B, S, d_model), dtype=jnp.float32)
        w_up = jax.random.normal(k2, (d_ff, d_model), dtype=jnp.float32) * 0.02
        w_down = jax.random.normal(k3, (d_model, d_ff), dtype=jnp.float32) * 0.02
        return {'x': x, 'w_up': w_up, 'w_down': w_down}
    _L1_ffn_in = _L1_ffn_setup()
    _d = {'L0_attn_x': _L0_attn_in['x'], 'L0_attn_w_qkv': _L0_attn_in['w_qkv'], 'L0_attn_b_qkv': _L0_attn_in['b_qkv'], 'L0_attn_w_out': _L0_attn_in['w_out'], 'L0_attn_b_out': _L0_attn_in['b_out'], 'L0_ffn_U1': _L0_ffn_in['U1'], 'L0_ffn_V1': _L0_ffn_in['V1'], 'L0_ffn_b1': _L0_ffn_in['b1'], 'L0_ffn_U2': _L0_ffn_in['U2'], 'L0_ffn_V2': _L0_ffn_in['V2'], 'L0_ffn_b2': _L0_ffn_in['b2'], 'L1_attn_Wqkv': _L1_attn_in['Wqkv'], 'L1_attn_bqkv': _L1_attn_in['bqkv'], 'L1_attn_Wr': _L1_attn_in['Wr'], 'L1_attn_br': _L1_attn_in['br'], 'L1_ffn_w_up': _L1_ffn_in['w_up'], 'L1_ffn_w_down': _L1_ffn_in['w_down']}
    _x0 = _d['L0_attn_x']
    _d['L0_attn_x'] = jax.random.normal(jax.random.fold_in(jax.random.key(seed), 1), (16, 512, 256), dtype=_x0.dtype)
    del _x0
    return _d

def reference(L0_attn_x, L0_attn_w_qkv, L0_attn_b_qkv, L0_attn_w_out, L0_attn_b_out, L0_ffn_U1, L0_ffn_V1, L0_ffn_b1, L0_ffn_U2, L0_ffn_V2, L0_ffn_b2, L1_attn_Wqkv, L1_attn_bqkv, L1_attn_Wr, L1_attn_br, L1_ffn_w_up, L1_ffn_w_down):

    def _L0_attn_ref(x, w_qkv, b_qkv, w_out, b_out):
        import jax, jax.numpy as jnp
        import numpy as np
        EMBED_DIM = 256
        NUM_HEADS = 16
        HEAD_DIM = EMBED_DIM // NUM_HEADS
        EPSILON = 1e-06
        SCORE_SCALE = 1.0
        B, L = (2, 512)
        Bq, Lq, E = x.shape
        qkv = x @ w_qkv + b_qkv
        q, k, v = jnp.split(qkv, 3, axis=-1)
        q = q.reshape(Bq, Lq, NUM_HEADS, HEAD_DIM).transpose(0, 2, 1, 3)
        k = k.reshape(Bq, Lq, NUM_HEADS, HEAD_DIM).transpose(0, 2, 1, 3)
        v = v.reshape(Bq, Lq, NUM_HEADS, HEAD_DIM).transpose(0, 2, 1, 3)
        dot = jnp.einsum('bhid,bhjd->bhij', q, k)
        q_norm_sq = jnp.sum(q * q, axis=-1, keepdims=True)
        k_norm_sq = jnp.sum(k * k, axis=-1, keepdims=True)
        vals = q_norm_sq + k_norm_sq.transpose(0, 1, 3, 2)
        scores = dot * dot / (vals - 2.0 * dot + EPSILON) * SCORE_SCALE
        mask = jnp.triu(jnp.ones((Lq, Lq), dtype=scores.dtype), k=1) * -1000000000.0
        scores = scores + mask[None, None, :, :]
        attn = jax.nn.softmax(scores, axis=-1)
        out = jnp.einsum('bhij,bhjd->bhid', attn, v)
        out = out.transpose(0, 2, 1, 3).reshape(Bq, Lq, E)
        return out @ w_out + b_out

    def _L0_ffn_ref(x, U1, V1, b1, U2, V2, b2):
        import jax, jax.numpy as jnp
        import numpy as np
        D_MODEL, D_FF, RANK = (256, 1024, 64)
        B, S = (4, 1024)
        P = jnp.einsum('bsd,dr->bsr', x, U1)
        H = jax.nn.gelu(jnp.einsum('bsr,rf->bsf', P, V1) + b1)
        Q = jnp.einsum('bsf,fr->bsr', H, U2)
        return jnp.einsum('bsr,rd->bsd', Q, V2) + b2

    def _L1_attn_ref(x, Wqkv, bqkv, Wr, br):
        import jax, jax.numpy as jnp
        import numpy as np
        B, C, D, H = (2, 512, 256, 16)
        HE = D // H
        b, c, d = x.shape
        h, he = (H, HE)
        xh = x.reshape(b, c, h, he).transpose(0, 2, 1, 3)
        qkv = jnp.einsum('bhce,ef->bhcf', xh, Wqkv) + bqkv
        q, k, v = jnp.split(qkv, 3, axis=-1)
        att = jnp.einsum('bhqe,bhke->bhqk', q, k) / jnp.sqrt(jnp.float32(he))
        mask = jnp.tril(jnp.ones((c, c), dtype=att.dtype), k=-1)
        att = jax.nn.softmax(att * mask, axis=-1)
        out = jnp.einsum('bhqk,bhke->bhqe', att, v)
        out = out.transpose(0, 2, 1, 3).reshape(b, c, d)
        out = out @ Wr + br
        return out

    def _L1_ffn_ref(x, w_up, w_down):
        import jax, jax.numpy as jnp
        import numpy as np
        EPS = 1e-08

        def _ternary_linear(x, w):
            alpha = jnp.mean(jnp.abs(w))
            w_t = jnp.sign(w) * (jnp.abs(w) > 0.5 * alpha).astype(w.dtype)
            w_q = w + jax.lax.stop_gradient(w_t - w)
            d = x.shape[-1]
            rms = jnp.sqrt(jnp.sum(x * x, axis=-1, keepdims=True)) / jnp.sqrt(jnp.asarray(d, x.dtype))
            x_norm = x / (rms + EPS)
            return jnp.einsum('bsd,fd->bsf', x_norm, w_q)
        h = jax.nn.gelu(_ternary_linear(x, w_up), approximate=False)
        return _ternary_linear(h, w_down)
    x = L0_attn_x
    x = x + _L0_attn_ref(_layernorm(x, axis=-1), L0_attn_w_qkv, L0_attn_b_qkv, L0_attn_w_out, L0_attn_b_out)
    x = x + _L0_ffn_ref(_layernorm(x, axis=-1), L0_ffn_U1, L0_ffn_V1, L0_ffn_b1, L0_ffn_U2, L0_ffn_V2, L0_ffn_b2)
    x = x + _L1_attn_ref(_layernorm(x, axis=-1), L1_attn_Wqkv, L1_attn_bqkv, L1_attn_Wr, L1_attn_br)
    x = x + _L1_ffn_ref(_layernorm(x, axis=-1), L1_ffn_w_up, L1_ffn_w_down)
    return x

_drawn_inputs = setup_inputs


def setup_inputs(seed=0):
    import zlib

    import numpy as np

    out = dict(_drawn_inputs(seed))
    spreads = {'L0_attn_b_qkv': (0.0, 0.1),
     'L0_attn_b_out': (0.0, 0.1),
     'L0_ffn_b1': (0.0, 0.8),
     'L0_ffn_b2': (0.0, 0.8)}
    factors = {'L0_ffn_U1': 8.0,
     'L0_ffn_V1': 8.0,
     'L0_ffn_U2': 8.0,
     'L0_ffn_V2': 8.0,
     'L1_attn_Wqkv': 8.0,
     'L1_attn_bqkv': 8.0,
     'L1_attn_Wr': 8.0,
     'L1_attn_br': 29.424}
    for name, (base, spread) in spreads.items():
        noise = np.random.default_rng([zlib.crc32(name.encode()), seed]).standard_normal(out[name].shape)
        drawn = base * np.exp(spread * noise) if base else spread * noise
        out[name] = jnp.asarray(drawn.astype(out[name].dtype))
    for name, factor in factors.items():
        out[name] = (out[name] * factor).astype(out[name].dtype)
    return out
```

```python
from contextlib import ExitStack

import numpy as np
import concourse.bass as bass
from concourse import mybir

F32 = mybir.dt.float32
BF16 = mybir.dt.bfloat16
ALU = mybir.AluOpType
ACT = mybir.ActivationFunctionType
AX_X = mybir.AxisListType.X

P = 128
ENGINES = ("pe", "act", "dve", "pool", "sp")

Q_PARTS = (0, 0, 1, 0, 2, 1)
K_PARTS = (0, 1, 0, 2, 0, 1)

MASK_SCORE = -1.0e9
MASK_DENOM = -1.0e18
MASK_DROP = -1.0e30


F_IDENT, F_TRI, F_ONES, F_NORM, F_COUNT = 0, 128, 256, 384, 392
F_COLS = 396
B_IDENT, B_DENOM, B_SCORE, B_MAX1, B_EXP1, B_PICK = 0, 128, 256, 384, 512, 640
B_COLS = 640 + 8 * 128


def constants():
    f = np.zeros((P, F_COLS), np.float32)
    i = np.arange(P)
    f[:, F_IDENT:F_IDENT + P] = np.eye(P)
    f[:, F_TRI:F_TRI + P] = i[:, None] >= i[None, :]
    f[:, F_ONES:F_ONES + P] = 1.0
    f[i, F_NORM + i // 16] = -0.5
    for t in range(4):
        f[:, F_COUNT + t] = 512 - (t * P + i)
    b = np.zeros((P, B_COLS), np.float32)
    row, col = i[:, None], i[None, :]
    b[:, B_IDENT:B_IDENT + P] = np.eye(P)
    b[:, B_DENOM:B_DENOM + P] = MASK_DENOM * (col > row)
    b[:, B_SCORE:B_SCORE + P] = MASK_SCORE * (row > col)
    b[:, B_MAX1:B_MAX1 + P] = MASK_DROP * (col >= row)
    b[:, B_EXP1:B_EXP1 + P] = MASK_DROP * (row >= col)
    for s in range(8):
        for part in range(3):
            b[part * 8 + s, B_PICK + s * P:B_PICK + (s + 1) * P] = 1.0
    return f, b


class Program:

    def __init__(self, nc, ctx):
        self.nc, self.ctx = nc, ctx
        self.queues = {e: [] for e in ENGINES}
        self.sems, self.counts, self.points = {}, {}, {}
        self.passed = {e: {} for e in ENGINES}
        self.phase = "start"

    def put(self, engine, name, key, waits, issue):
        if name not in self.sems:
            self.sems[name] = self.ctx.enter_context(self.nc.semaphore(name))
            self.counts[name] = 0
        self.counts[name] += 16 if name.startswith("dma_") else 1
        self.points[self.phase, name, key] = (name, self.counts[name])
        self.queues[engine].append((waits, issue, name))

    def on(self, name, key, phase=None):
        first = key[0] if isinstance(key, tuple) else key
        return None if first < 0 else self.points[phase or self.phase, name, key]

    def all_of(self, name):
        return (name, self.counts[name])

    def emit(self, engine, eng):
        passed = self.passed[engine]
        for waits, issue, name in self.queues[engine]:
            for wait in waits:
                if wait is not None and passed.get(wait[0], 0) < wait[1]:
                    eng.wait_ge(self.sems[wait[0]], wait[1])
                    passed[wait[0]] = wait[1]
            issue(eng).then_inc(self.sems[name], 16 if name.startswith("dma_") else 1)
        self.queues[engine] = []

    def run_block(self):
        with self.nc.Block() as block:
            @block.sync
            def _(e):
                self.emit("sp", e)

            @block.scalar
            def _(e):
                self.emit("act", e)

            @block.vector
            def _(e):
                self.emit("dve", e)

            @block.gpsimd
            def _(e):
                self.emit("pool", e)

            @block.tensor
            def _(e):
                self.emit("pe", e)


class Steps:

    def __init__(self):
        self.tasks = []

    def step(self):
        if self.tasks and next(self.tasks[0], StopIteration) is StopIteration:
            self.tasks.pop(0)

    def all(self):
        while self.tasks:
            self.step()


class Net:

    def __init__(self, nc, ctx, B, L, D):
        self.nc, self.B, self.L, self.D = nc, B, L, D
        self.T = L // P
        self.program = Program(nc, ctx)
        sb = lambda n, s, d=F32: ctx.enter_context(nc.sbuf_tensor(n, s, d))
        self.x = sb("x", [P, B * self.T, D])
        self.cf = sb("const_f_sb", [P, F_COLS])
        self.cb = sb("const_b_sb", [P, B_COLS], BF16)
        self.eps_ln = sb("eps_ln", [P, 1])
        self.eps_ratio = sb("eps_ratio", [P, 1])
        self.stats6 = sb("stats6", [P, self.T, 6])
        self.mean_var = sb("mean_var", [P, B * self.T, 2])
        self.rstd = sb("rstd", [P, B * self.T])
        self.banks = [ctx.enter_context(nc.psum_tensor(f"bank{i}", [P, 512], F32)) for i in range(8)]
        self.ident = self.cf[:, F_IDENT:F_IDENT + P]
        self.ones = self.cf[:, F_ONES:F_ONES + P]
        self.ident_b = self.cb[:, B_IDENT:B_IDENT + P]
        self.stats_made = None

    def xb(self, b):
        return self.x[:, b * self.T:(b + 1) * self.T, :]

    def mask(self, at):
        return self.cb[:, at:at + P]


class Phase:

    def __init__(self, net, kind):
        self.net, self.pr, self.kind = net, net.program, kind
        self.pr.phase = kind
        self.on, self.put = self.pr.on, self.pr.put


def row_stats(net, b, of, x_made):
    pr, T = net.program, net.T
    def stats(e):
        for t in range(T):
            i = e.bn_stats(net.stats6[:, t, :], net.x[:, b * T + t, :])
        return i
    pr.put("dve", "bn_stats", (b, of), [x_made, net.stats_made], stats)
    def aggregate(e):
        for t in range(T):
            i = e.bn_aggr(net.mean_var[:, b * T + t, :], net.stats6[:, t, :])
        return i
    pr.put("dve", "bn_aggr", (b, of), [pr.on("bn_stats", (b, of))], aggregate)
    net.stats_made = pr.on("bn_aggr", (b, of))


def turn_blocks(e, bank, src_of, pair, ident):
    for tt in range(2):
        for c in range(2):
            i = e.transpose(bank[:, c * 256 + tt * P:c * 256 + (tt + 1) * P],
                            src_of(2 * pair + tt)[:, c * P:(c + 1) * P], ident)
    return i


def load_row(net, x_dram, b):
    source = x_dram[b].rearrange("(t p) d -> p t d", p=P)
    net.program.put("sp", f"dma_x{b}", 0, [], lambda e: e.dma_start(net.xb(b), source))


def load_start(net, x_dram, cf_dram, cb_dram, weights):
    pr, nc = net.program, net.nc
    with nc.sbuf_tensor("stage_b", [P, B_COLS], F32) as stage:
        load_row(net, x_dram, 0)
        pr.put("sp", "dma_const_b", 0, [], lambda e: e.dma_start(stage[:, :], cb_dram))
        pr.put("sp", "dma_const_f", 0, [], lambda e: e.dma_start(net.cf[:, :], cf_dram))
        weights.load()
        for b in range(1, net.B):
            load_row(net, x_dram, b)
        pr.put("dve", "const_b", 0, [pr.on("dma_const_b", 0), pr.on("dma_const_f", 0)],
               lambda e: e.tensor_copy(net.cb[:, :], stage[:, :]))
        pr.put("dve", "eps", 0, [], lambda e: e.memset(net.eps_ln[:, :], 1e-5))
        pr.put("dve", "eps", 1, [], lambda e: e.memset(net.eps_ratio[:, :], 1e-6))
        pr.run_block()



H, HD = 16, 16
HALF = 8
GROUP = 4
STACK = 6 * HD
TWO_ONES = float(np.array([0x3F803F80], np.uint32).view(np.float32)[0])
NORM_ROWS = 3


def units_of_group():
    out = []
    for pair in range(2):
        h0, h1 = 2 * pair, 2 * pair + 1
        for h in (h0, h1):
            out.append([(h, 3, 0)])
            out.append([(h, 2, 0), (h, 0, 384)])
        out.append([(h0, 1, 0), (h1, 1, 256)])
    return out


UNITS = units_of_group()
N_UNITS = len(UNITS)
PAIR_UNITS = N_UNITS // 2
HALF_UNITS = 2 * N_UNITS
WHERE = {(h, ib): (u, off) for u, segs in enumerate(UNITS) for h, ib, off in segs}
ATTEND = ((3,), (2,), (1, 0))

BACK_LAG = 10
TURN_SLOT = 3
GATHER_SLOT = 14
VALUES_SLOT = BACK_LAG + 5
S_BUFS, INV_BUFS, PROB_BUFS = 11, 3, 13
M_BUFS = 5


def width(segs):
    return max(off + (ib + 1) * P for _, ib, off in segs)


def m_col(h, ib):
    return (h % 2) * 4 + ib


class AttentionWeights:

    def __init__(self, net, ctx, kind, args):
        self.net, self.kind, self.args = net, kind, args
        sb = lambda n, s: ctx.enter_context(net.nc.sbuf_tensor(f"{kind}_{n}", s, F32))
        D = net.D
        ratio = kind == "ratio"
        self.w_in = sb("w_in", [P, 2, 3 * D] if ratio else [P, 3, P])
        self.bias_qk = sb("bias_qk", [P, 4 if ratio else 2])
        self.bias_v = sb("bias_v", [P, D])
        self.bias_o = sb("bias_o", [P, D])
        self.w_o = sb("w_o", [P, 2, D])

    def load(self):
        args, D, pr, name = self.args, self.net.D, self.net.program, f"dma_{self.kind}_weights"
        n = [0]
        def load(dst, src, waits=(), slow=False):
            pr.put("sp", name, n[0], list(waits), lambda e: e.dma_start(
                dst, src, allow_slow_non_contiguous=True) if slow else e.dma_start(dst, src))
            n[0] += 1
        if self.kind == "ratio":
            load(self.w_in[:, :, :], args["w_in"].rearrange("(c p) n -> p c n", p=P))
            load(self.bias_qk[:, :], args["b_in"][0:2 * D].rearrange("(c p) -> p c", p=P), slow=True)
            load(self.bias_v[:, :], args["b_in"][2 * D:3 * D].partition_broadcast(P))
        else:
            pr.put("dve", "w_zero", 0, [], lambda e: e.memset(self.w_in[:, :, :], 0.0))
            for h in range(HALF):
                r = slice(h * HD, (h + 1) * HD)
                load(self.w_in[r, :, r], args["w_in"].rearrange("e (k d) -> e k d", k=3), [pr.on("w_zero", 0)])
                load(self.bias_qk[r, :], args["b_in"][0:2 * HD].rearrange("(k d) -> d k", k=2), slow=True)
            for h in range(H):
                load(self.bias_v[:, h * HD:(h + 1) * HD], args["b_in"][2 * HD:3 * HD].partition_broadcast(P))
        load(self.w_o[:, :, :], args["w_o"].rearrange("(c p) n -> p c n", p=P))
        load(self.bias_o[:, :], args["b_o"].partition_broadcast(P))
        self.loaded = pr.on(name, n[0] - 1)


class Attention(Phase):
    def __init__(self, net, ctx, kind, w):
        super().__init__(net, kind)
        self.w_in, self.bias_qk, self.bias_v, self.bias_o, self.w_o = w.w_in, w.bias_qk, w.bias_v, w.bias_o, w.w_o
        self.weights = w.loaded
        nc = net.nc
        sb = lambda n, s, d=F32: ctx.enter_context(nc.sbuf_tensor(f"{kind}_{n}", s, d))
        self.ratio = kind == "ratio"
        L, D, T = net.L, net.D, net.T
        self.qs = sb("q_stack", [P, 2, HALF, L], BF16)
        self.ks = sb("k_stack", [P, 2, HALF, L], BF16)
        self.xnT = sb("xn_T", [P, 2, L])
        self.xn = sb("xn", [P, 2, D])
        self.parts = sb("parts", [P, 2, 3, L], BF16)
        self.rest = sb("rest", [P, 2, L])
        self.values_ones = sb("v_ones", [P, 2, T, HALF, 32])
        self.prob = sb("prob", [P, PROB_BUFS, L])
        self.o_group = sb("o_group", [P, 2, L])
        self.o_tok = sb("o_tok", [P, T, D])
        self.oT = sb("o_T", [P, 2, L // 2])
        self.rec = sb("rec_den", [P, T, GROUP])
        self.mx = sb("max_cols", [P, M_BUFS, 8])
        self.neg = sb("neg_max", [P, M_BUFS, 8])
        self.m_rest = sb("m_rest", [P, 2, 8])
        self.m_parts = sb("m_parts", [P, M_BUFS, 3, 8], BF16)
        self.mT = sb("m_T", [24, M_BUFS, P], BF16)
        if self.ratio:
            self.sq = sb("squares", [P, L])
            self.n_parts = sb("n_parts", [HALF, 3, L], BF16)
            self.inv = sb("inv_root", [P, INV_BUFS, L])
            self.scores = sb("scores", [P, S_BUFS, L])
        else:
            self.v_flat = sb("v_flat", [P, T, D])
            self.suffix = sb("v_suffix", [P, 2, T, D])
            self.c_masked = sb("c_masked", [P, M_BUFS, 8])
            self.num = sb("numer", [P, 2, T, GROUP, HD])
            self.c_cnt = sb("c_count", [P, 2, T, GROUP])
        dram = lambda n, s: nc.dram_tensor(f"{kind}_{n}", s, BF16, kind="Internal").ap()
        self.part_dram = [[dram(f"parts_{s}{i}", [3, P, L]) for i in range(2)] for s in "qk"]
        self.norm_dram = [[dram(f"norms_{s}{i}", [3, HALF, L]) for i in range(2)] for s in "qk"]
        bk = net.banks
        if self.ratio:
            self.den_bank, self.dot_banks = bk[0], bk[1:3]
        else:
            self.dot_banks = bk[0:3]
        self.exp_banks, self.o_bank = bk[3:5], bk[5]
        self.side_banks, self.side_turn, self.side_empty = bk[6:8], 1, [None, None]

    def next_side(self):
        self.side_turn = 1 - self.side_turn
        return self.side_banks[self.side_turn], self.side_turn

    def set_ones(self):
        if self.ratio:
            pairs = lambda stack: stack[STACK:P, :, :, :].rearrange("p s h t -> p (s h t)").bitcast(F32)
            self.put("dve", "q_ones", 0, [], lambda e: e.memset(pairs(self.qs), TWO_ONES))
            self.put("pool", "k_ones", 0, [], lambda e: e.memset(pairs(self.ks), TWO_ONES))
        self.put("pool", "v_ones", 0, [self.on("k_ones", 0) if self.ratio else None], lambda e: e.memset(self.values_ones[:, :, :, :, HD:32], 1.0))

    def normalise(self, b):
        net, T = self.net, self.net.T
        cols = slice(b * T, (b + 1) * T)
        loaded = self.on(f"dma_x{b}", 0, "start") if self.ratio else None
        row_stats(net, b, "input", loaded)
        stats = self.on("bn_aggr", (b, "input"))
        self.put("act", "log_var", b, [stats], lambda e: e.activation(
            net.rstd[:, cols], net.mean_var[:, cols, 1], ACT.Ln, bias=net.eps_ln[:, :]))
        self.put("act", "rstd", b, [self.on("log_var", b)], lambda e: e.activation(
            net.rstd[:, cols], net.rstd[:, cols], ACT.Exp, scale=-0.5))
        yield
        for pair in range(T // 2):
            before = self.on("xn_turned", (b, 0)) if pair else self.on("xn_turned", (b - 1, T // 2 - 1))
            def normal(e, pair=pair):
                for tt in range(2):
                    t = b * T + 2 * pair + tt
                    i = e.tensor_scalar(self.xn[:, tt, :], net.x[:, t, :], net.mean_var[:, t, 0:1],
                                        net.rstd[:, t:t + 1], ALU.subtract, ALU.mult)
                return i
            self.put("dve", "xn", (b, pair), [before, self.on("rstd", b), stats, loaded], normal)
            yield
            bank, k = self.next_side()
            self.put("pe", "xn_turned", (b, pair), [self.side_empty[k], self.on("xn", (b, pair))],
                     lambda e, pair=pair, bank=bank: turn_blocks(e, bank, lambda t: self.xn[:, t % 2, :], pair, net.ident))
            in_use = [self.on("v_made", (2 * b - 1, T // 2 - 1)), self.on("projected", (2 * b - 1, 1))]
            self.put("act", "xnT", (b, pair), [self.on("xn_turned", (b, pair))] + in_use,
                     lambda e, pair=pair, bank=bank: e.activation(
                         self.xnT[:, :, pair * 256:(pair + 1) * 256],
                         bank[:, :].rearrange("p (c t) -> p c t", c=2), ACT.Copy))
            self.side_empty[k] = self.on("xnT", (b, pair))

    def split(self, half, side):
        b, m = divmod(half, 2)
        D = self.net.D
        bank, k = self.next_side()
        key = (half, side)
        def project(e):
            if not self.ratio:
                return e.matmul(bank[:, :], self.w_in[:, side, :], self.xnT[:, m, :], start=True, stop=True)
            for c in range(2):
                lo = side * D + m * P
                i = e.matmul(bank[:, :], self.w_in[:, c, lo:lo + P], self.xnT[:, c, :],
                             start=(c == 0), stop=(c == 1))
            return i
        self.put("pe", "projected", key, [self.side_empty[k], self.on("xnT", (b, 1)), self.weights], project)
        bias = self.bias_qk[:, 2 * side + m:2 * side + m + 1] if self.ratio else self.bias_qk[:, side:side + 1]
        p = side
        sent = self.on(f"dma_parts{side}", half - 1)
        self.put("act", "hi", key, [self.on("projected", key), self.weights, sent], lambda e: e.activation(
            self.parts[:, p, 0, :], bank[:, :], ACT.Identity, bias=bias))
        if self.ratio:
            done = self.on("norm_rows", (half, 0) if side else (half - 1, 1))
            self.put("act", "squares", key, [done], lambda e: e.activation(
                self.sq[:, :], bank[:, :], ACT.Square, bias=bias))
        before = (half, 0) if side else (half - 1, 1)
        self.put("dve", "rest", key,
                 [self.on("squares" if self.ratio else "hi", key), self.on("lo", before)],
                 lambda e: e.scalar_tensor_tensor(
                     out=self.rest[:, 0, :], in0=bank[:, :], scalar=bias, in1=self.parts[:, p, 0, :],
                     op0=ALU.add, op1=ALU.subtract))
        self.side_empty[k] = self.on("rest", key)
        self.put("dve", "mid", key, [self.on("rest", key), sent], lambda e: e.tensor_copy(
            self.parts[:, p, 1, :], self.rest[:, 0, :]))
        self.put("pool", "lo", key, [self.on("mid", key)], lambda e: e.tensor_tensor(
            self.parts[:, p, 2, :], self.rest[:, 0, :], self.parts[:, p, 1, :], ALU.subtract))
        dst = self.part_dram[side][half % 2]
        self.put("sp", f"dma_parts{side}", half,
                 [self.on("lo", key), self.on("hi", key), None if half < 2 else self.gathered[half - 2]],
                 lambda e: e.dma_start(dst.rearrange("r p t -> p r t"), self.parts[:, p, :, :]))

    def norms(self, half, side):
        net = self.net
        key = (half, side)
        bank, k = self.next_side()
        self.put("pe", "norm_rows", key, [self.side_empty[k], self.on("squares", key)], lambda e: e.matmul(
            bank[0:HALF, :], net.cf[:, F_NORM:F_NORM + HALF], self.sq[:, :], start=True, stop=True))
        sent = self.on("dma_norms0", half) if side else self.on("dma_norms1", half - 1)
        self.put("act", "norm_hi", key, [self.on("norm_rows", key), sent], lambda e: e.activation(
            self.n_parts[:, 0, :], bank[0:HALF, :], ACT.Copy))
        rest = self.rest[0:HALF, 1, :]
        before = self.on("norm_lo", (half, 0) if side else (half - 1, 1))
        self.put("dve", "norm_rest", key, [self.on("norm_hi", key), before],
                 lambda e: e.tensor_tensor(rest, bank[0:HALF, :], self.n_parts[:, 0, :], ALU.subtract))
        self.side_empty[k] = self.on("norm_rest", key)
        self.put("dve", "norm_mid", key, [self.on("norm_rest", key), sent], lambda e: e.tensor_copy(
            self.n_parts[:, 1, :], rest))
        self.put("pool", "norm_lo", key, [self.on("norm_mid", key)], lambda e: e.tensor_tensor(
            self.n_parts[:, 2, :], rest, self.n_parts[:, 1, :], ALU.subtract))
        dst = self.norm_dram[side][half % 2]
        self.put("sp", f"dma_norms{side}", half,
                 [self.on("norm_lo", key), None if half < 2 else self.gathered[half - 2]],
                 lambda e: e.dma_start(dst.rearrange("r h t -> h r t"), self.n_parts[:, :, :]))

    def values(self, half, pair):
        net, D = self.net, self.net.D
        b, m = divmod(half, 2)
        key, vs = (half, pair), half % 2
        bank, k = self.next_side()
        def make(e):
            for tt in range(2):
                t = 2 * pair + tt
                out = bank[:, tt * P:(tt + 1) * P]
                if not self.ratio:
                    i = e.matmul(out, self.xnT[:, m, t * P:(t + 1) * P], self.w_in[:, 2, :], start=True, stop=True)
                    continue
                for c in range(2):
                    i = e.matmul(out, self.xnT[:, c, t * P:(t + 1) * P],
                                 self.w_in[:, c, 2 * D + m * P:2 * D + (m + 1) * P],
                                 start=(c == 0), stop=(c == 1))
            return i
        self.put("pe", "v_made", key, [self.side_empty[k], self.on("xnT", (b, 1)), self.weights], make)
        by_head = lambda a: a.rearrange("p (h d) -> p h d", h=HALF)
        def add(e):
            for tt in range(2):
                i = e.tensor_tensor(self.values_ones[:, vs, 2 * pair + tt, :, 0:HD], by_head(bank[:, tt * P:(tt + 1) * P]),
                                    by_head(self.bias_v[:, m * P:(m + 1) * P]), ALU.add)
            return i
        in_use = [self.on("attended", (2 * half - 3, 2))]
        if not self.ratio:
            in_use.append(self.on("v_flat", (half - 2, pair)))
        self.put("dve", "v_ready", key, [self.on("v_made", key), self.on("v_ones", 0), self.weights] + in_use, add)
        self.side_empty[k] = self.on("v_ready", key)
        if not self.ratio:
            def flat(e):
                for tt in range(2):
                    t = 2 * pair + tt
                    i = e.tensor_copy(by_head(self.v_flat[:, t, m * P:(m + 1) * P]), self.values_ones[:, vs, t, :, 0:HD])
                return i
            self.put("pool", "v_flat", key, [self.on("v_ready", key), self.on("suffix", (b - 1, 1))], flat)

    def suffix_sums(self, b, pair):
        net, T = self.net, self.net.T
        key = (b, pair)
        bank, k = self.next_side()
        def make(e):
            for tt in range(2):
                ib = 2 * pair + tt
                for jb in range(ib, T):
                    upper = net.cf[:, F_TRI:F_TRI + P] if jb == ib else net.ones
                    i = e.matmul(bank[:, tt * 256:(tt + 1) * 256], upper, self.v_flat[:, jb, :],
                                 start=(jb == ib), stop=(jb == T - 1))
            return i
        self.put("pe", "suffix", key, [self.side_empty[k], self.on("v_flat", (2 * b + 1, 1))], make)
        self.put("act", "suffix_copy", key, [self.on("suffix", key), self.on("masked_part", 4 * (b - 2) + 3)],
                 lambda e: e.activation(self.suffix[:, b % 2, 2 * pair:2 * pair + 2, :],
                                        bank[:, :].rearrange("p (t d) -> p t d", t=2), ACT.Copy))
        self.side_empty[k] = self.on("suffix_copy", key)

    def prepare(self, half):
        b, m = divmod(half, 2)
        if m == 0:
            yield from self.normalise(b)
            yield
        for side in range(2):
            self.split(half, side)
            yield
            if self.ratio:
                self.norms(half, side)
                yield

    def prepare_values(self, half):
        b, m = divmod(half, 2)
        for pair in range(2):
            self.values(half, pair)
            yield
        if not self.ratio and m == 1:
            for pair in range(2):
                self.suffix_sums(b, pair)
                yield

    def gather(self, half):
        s = half % 2
        sent = [self.on(f"dma_parts{side}", half) for side in range(2)]
        if self.ratio:
            sent += [self.on(f"dma_norms{side}", half) for side in range(2)]
        last = (half - 1) * HALF_UNITS - 1
        in_use = [self.on("dots", last), self.on("denoms" if self.ratio else "shifted", last)]
        ones = [self.on("q_ones", 0), self.on("k_ones", 0)] if self.ratio else []
        name, n = f"dma_gathered{s}", 0
        for dst, side, order in ((self.qs, 0, Q_PARTS), (self.ks, 1, K_PARTS)):
            for strip, part in enumerate(order):
                src = self.part_dram[side][s][part].rearrange("(h d) t -> d h t", d=HD)
                self.put("sp", name, (half, n), sent + in_use, lambda e, dst=dst, strip=strip, src=src: e.dma_start(
                    dst[strip * HD:(strip + 1) * HD, s, :, :], src))
                n += 1
            if self.ratio:
                at = STACK + side * NORM_ROWS
                self.put("sp", name, (half, n), sent + in_use + ones, lambda e, dst=dst, at=at, side=side: e.dma_start(
                    dst[at:at + NORM_ROWS, s, :, :], self.norm_dram[side][s]))
                n += 1
        self.gathered[half] = self.on(name, (half, n - 1))

    def product(self, e, n, bank, rows, mask):
        g, u = divmod(n, N_UNITS)
        s = (g // 2) % 2
        for k, (h, ib, off) in enumerate(UNITS[u]):
            w, hh = (ib + 1) * P, (g % 2) * GROUP + h
            i = e.matmul(bank[:, off:off + w], self.qs[0:rows, s, hh, ib * P:(ib + 1) * P],
                         self.ks[0:rows, s, hh, 0:w], start=(k == 0), stop=mask is None, skip_group_check=True)
            if mask is not None:
                i = e.matmul(bank[:, off + w - P:off + w], self.net.ident_b, self.net.mask(mask),
                             start=False, stop=True, skip_group_check=True)
        return i

    def inverse_root(self, n):
        w, half = width(UNITS[n % N_UNITS]), n // HALF_UNITS
        self.put("pe", "denoms", n, [self.gathered[half], self.on("log_den", n - 1)],
                 lambda e: self.product(e, n, self.den_bank, STACK + 2 * NORM_ROWS, B_DENOM))
        inv = self.inv[:, n % INV_BUFS, 0:w]
        self.put("act", "log_den", n, [self.on("denoms", n), self.on("ratio", n - INV_BUFS)], lambda e: e.activation(
            inv, self.den_bank[:, 0:w], ACT.Ln, scale=-2.0, bias=self.net.eps_ratio[:, :]))
        self.put("act", "inv_root", n, [self.on("log_den", n)], lambda e: e.activation(
            inv, inv, ACT.Exp, scale=-0.5))

    def front(self, n, split):
        segs, half, pair = UNITS[n % N_UNITS], n // HALF_UNITS, n // PAIR_UNITS
        w, ms = width(segs), pair % M_BUFS
        bank = self.dot_banks[n % len(self.dot_banks)]
        m_free = self.on("m_neg", pair - M_BUFS)
        if not self.ratio:
            self.put("pe", "dots", n, [self.gathered[half], self.on("maxima", n - 3)],
                     lambda e: self.product(e, n, bank, STACK, B_MAX1))
            def maxima(e):
                for h, ib, off in segs:
                    c = m_col(h, ib)
                    i = e.tensor_reduce(self.mx[:, ms, c:c + 1], bank[:, off:off + (ib + 1) * P], AX_X, ALU.max)
                return i
            self.put("dve", "maxima", n, [self.on("dots", n), m_free], maxima)
            split.step()
            return
        self.put("pe", "dots", n, [self.gathered[half], self.on("ratio", n - 2)],
                 lambda e: self.product(e, n, bank, STACK, None))
        s = self.scores[:, n % S_BUFS, :]
        self.put("dve", "ratio", n, [self.on("dots", n), self.on("inv_root", n), self.on("shifted", n - S_BUFS)],
                 lambda e: e.tensor_tensor(s[:, 0:w], bank[:, 0:w], self.inv[:, n % INV_BUFS, 0:w], ALU.mult))
        split.step()
        def squares(e):
            for h, ib, off in segs:
                seg, c = s[:, off:off + (ib + 1) * P], m_col(h, ib)
                i = e.tensor_tensor_reduce(seg, seg, seg, 1.0, 0.0, ALU.mult, ALU.max, self.mx[:, ms, c:c + 1])
            return i
        self.put("dve", "maxima", n, [self.on("ratio", n), m_free], squares)

    def split_maxima(self, pair):
        ms = pair % M_BUFS
        mx, neg = self.mx[:, ms, :], self.neg[:, ms, :]
        part = lambda k: self.m_parts[:, ms, k, :]
        rest = lambda k: self.m_rest[:, k, :]
        last = self.on("maxima", (pair + 1) * PAIR_UNITS - 1)
        turned = self.on("m_turned", pair - M_BUFS)
        if self.ratio:
            self.put("dve", "m_neg", pair, [last], lambda e: e.tensor_scalar(neg, mx, -1.0, None, ALU.mult))
        else:
            self.put("dve", "m_neg", pair, [last, self.on("c_masked", pair - M_BUFS)],
                     lambda e: e.tensor_scalar(neg, mx, 0.0, -1.0, ALU.max, ALU.mult))
            group = (pair - M_BUFS) // 2
            self.put("act", "c_masked", pair, [self.on("m_neg", pair), self.on("masked_part", group)],
                     lambda e: e.activation(self.c_masked[:, ms, :], neg, ACT.Exp, scale=0.25))
        yield
        self.put("dve", "m_hi", pair, [self.on("m_neg", pair), turned], lambda e: e.tensor_copy(part(0), neg))
        yield
        self.put("dve", "m_rest0", pair, [self.on("m_hi", pair)], lambda e: e.tensor_tensor(
            rest(0), neg, part(0), ALU.subtract))
        yield
        self.put("dve", "m_mid", pair, [self.on("m_rest0", pair)], lambda e: e.tensor_copy(part(1), rest(0)))
        yield
        self.put("dve", "m_rest1", pair, [self.on("m_mid", pair)], lambda e: e.tensor_tensor(
            rest(1), rest(0), part(1), ALU.subtract))
        yield
        self.put("dve", "m_lo", pair, [self.on("m_rest1", pair)], lambda e: e.tensor_copy(part(2), rest(1)))

    def turn_maxima(self, pair):
        ms = pair % M_BUFS
        side, k = self.next_side()
        bank = side[0:24, 0:P // 2].bitcast(BF16)
        self.put("pe", "m_turned", pair, [self.on("m_lo", pair), self.side_empty[k]], lambda e: e.transpose(
            bank, self.m_parts[:, ms, :, :].rearrange("p r s -> p (r s)"), self.net.ident_b))
        self.put("dve", "m_rows", pair, [self.on("m_turned", pair), self.on("shifted", (pair + 1 - M_BUFS) * PAIR_UNITS - 1)],
                 lambda e: e.tensor_copy(self.mT[:, ms, :], bank))
        self.side_empty[k] = self.on("m_rows", pair)

    def back(self, n):
        net = self.net
        g, u = divmod(n, N_UNITS)
        segs, pair, st = UNITS[u], n // PAIR_UNITS, (g // 2) % 2
        w_all, ms = width(segs), pair % M_BUFS
        bank = self.exp_banks[n % 2]

        def make(e):
            first = True
            for h, ib, off in segs:
                w, hh, c = (ib + 1) * P, (g % 2) * GROUP + h, m_col(h, ib)
                for jb in range(ib + 1):
                    at = slice(off + jb * P, off + (jb + 1) * P)
                    if self.ratio:
                        e.matmul(bank[:, at], self.scores[:, n % S_BUFS, at], net.ident,
                                 is_transpose=True, start=first, stop=False, skip_group_check=True)
                    else:
                        e.matmul(bank[:, at], self.ks[0:STACK, st, hh, jb * P:(jb + 1) * P],
                                 self.qs[0:STACK, st, hh, ib * P:(ib + 1) * P],
                                 start=first, stop=False, skip_group_check=True)
                    first = False
                e.matmul(bank[:, off:off + w], net.cb[0:24, B_PICK + c * P:B_PICK + (c + 1) * P],
                         self.mT[:, ms, :].unsqueeze(1).to_broadcast([24, ib + 1, P]),
                         start=False, stop=False, skip_group_check=True)
                i = e.matmul(bank[:, off + w - P:off + w], net.ident_b, net.mask(B_SCORE if self.ratio else B_EXP1),
                             start=False, stop=True, skip_group_check=True)
            return i

        scores = self.on("maxima", n) if self.ratio else self.gathered[g // 2]
        self.put("pe", "shifted", n, [scores, self.on("m_rows", pair), self.on("prob", n - 2)], make)
        old = n - PROB_BUFS
        in_use = self.on("attended", self.attended_by(old)) if old >= 0 else None
        self.put("act", "prob", n, [self.on("shifted", n), in_use], lambda e: e.activation(
            self.prob[:, n % PROB_BUFS, 0:w_all], bank[:, 0:w_all], ACT.Exp, scale=1.0 if self.ratio else 0.25))

    def attended_by(self, n):
        g, u = divmod(n, N_UNITS)
        part = max(k for k, blocks in enumerate(ATTEND) for _, ib, _ in UNITS[u] if ib in blocks)
        return (g, part)

    def attend(self, g, part):
        vs, base = (g // 2) % 2, g * N_UNITS
        def make(e):
            for ib in ATTEND[part]:
                for jb in range(ib + 1):
                    for h in range(GROUP):
                        u, off = WHERE[h, ib]
                        i = e.matmul(self.o_bank[32 * h:32 * h + 32, ib * P:(ib + 1) * P],
                                     self.values_ones[:, vs, jb, (g % 2) * GROUP + h, :],
                                     self.prob[:, (base + u) % PROB_BUFS, off + jb * P:off + (jb + 1) * P],
                                     start=(jb == 0), stop=(jb == ib), skip_group_check=True)
            return i
        self.put("pe", "attended", (g, part),
                 [self.on("prob", base + N_UNITS - 1), self.on("v_ready", (g // 2, 1)), self.on("o_group", g - 1)], make)

    def evacuate(self, g):
        T = self.net.T
        waits = [self.on("attended", (g, 2)), self.on("o_turned", g - 2)]
        if self.ratio:
            self.put("dve", "o_group", g, waits, lambda e: e.tensor_copy(self.o_group[:, g % 2, :], self.o_bank[:, :]))
        else:
            self.put("act", "o_group", g, waits, lambda e: e.activation(
                self.o_group[:, g % 2, :], self.o_bank[:, :], ACT.Copy))
        if self.ratio:
            return
        b, gb = divmod(g, 4)
        nr = g % 2
        def masked(e):
            for k in range(2):
                c = self.c_masked[:, (2 * g + k) % M_BUFS, :].rearrange("p (h t) -> p t h", h=2)
                sums = self.suffix[:, b % 2, :, gb * 64 + k * 32:gb * 64 + (k + 1) * 32]
                e.tensor_tensor(self.num[:, nr, :, 2 * k:2 * k + 2, :], sums.rearrange("p t (h d) -> p t h d", h=2),
                                c.unsqueeze(3).to_broadcast([P, T, 2, HD]), ALU.mult)
                i = e.tensor_tensor(self.c_cnt[:, nr, :, 2 * k:2 * k + 2], c,
                                    self.net.cf[:, F_COUNT:F_COUNT + T].unsqueeze(2).to_broadcast([P, T, 2]),
                                    ALU.mult)
            return i
        self.put("pool", "masked_part", g,
                 [self.on("c_masked", 2 * g + 1), self.on("suffix_copy", (b, 1)), self.on("o_tok", g - 2)], masked)

    def finish_group(self, g):
        net, T = self.net, self.net.T
        b, gb = divmod(g, 4)
        bank, k = self.next_side()
        def turn(e):
            for t in range(T):
                i = e.transpose(bank[:, t * P:(t + 1) * P], self.o_group[:, g % 2, t * P:(t + 1) * P], net.ident)
            return i
        self.put("pe", "o_turned", g, [self.side_empty[k], self.on("o_group", g)], turn)
        view = bank[:, :].rearrange("p (t h c) -> p t h c", t=T, h=GROUP)
        out = self.o_tok[:, :, gb * 64:(gb + 1) * 64].rearrange("p t (h d) -> p t h d", h=GROUP)
        rec = self.rec[:, :, :]
        rec_b = rec.unsqueeze(3).to_broadcast([P, T, GROUP, HD])
        tok_free = self.on("ot_turned", (b - 1, 1))
        if self.ratio:
            self.put("dve", "rec_den", g, [self.on("o_turned", g), self.on("o_tok", g - 1)],
                     lambda e: e.reciprocal(rec, view[:, :, :, HD]))
            self.put("dve", "o_tok", g, [self.on("rec_den", g), tok_free], lambda e: e.tensor_tensor(
                out, view[:, :, :, 0:HD], rec_b, ALU.mult))
            self.side_empty[k] = self.on("o_tok", g)
        else:
            num, cnt = self.num[:, g % 2, :, :, :], self.c_cnt[:, g % 2, :, :]
            self.put("dve", "den_sum", g, [self.on("o_turned", g), self.on("masked_part", g), self.on("o_tok", g - 1)],
                     lambda e: e.tensor_tensor(rec, view[:, :, :, HD], cnt, ALU.add))
            self.put("dve", "num_sum", g, [self.on("o_turned", g), self.on("masked_part", g)],
                     lambda e: e.tensor_tensor(num, view[:, :, :, 0:HD], num, ALU.add))
            self.side_empty[k] = self.on("num_sum", g)
            self.put("dve", "rec_den", g, [self.on("den_sum", g)], lambda e: e.reciprocal(rec, rec))
            self.put("dve", "o_tok", g, [self.on("rec_den", g), self.on("num_sum", g), tok_free],
                     lambda e: e.tensor_tensor(out, num, rec_b, ALU.mult))
        yield
        if gb == 3:
            yield from self.finish_row(b)

    def finish_row(self, b):
        net, T, D = self.net, self.net.T, self.net.D
        self.put("pool", "x_bias", b, [self.weights, self.on("xn", (b, 1))], lambda e: e.tensor_tensor(
            net.xb(b), net.xb(b), self.bias_o[:, :].unsqueeze(1).to_broadcast([P, T, D]), ALU.add))
        for pair in range(T // 2):
            key = (b, pair)
            bank, k = self.next_side()
            self.put("pe", "ot_turned", key, [self.side_empty[k], self.on("o_tok", 4 * b + 3)],
                     lambda e, pair=pair, bank=bank: turn_blocks(e, bank, lambda t: self.o_tok[:, t, :], pair, net.ident))
            before = self.on("out_proj", (b, 0) if pair else (b - 1, 1))
            self.put("act", "oT", key, [self.on("ot_turned", key), before],
                     lambda e, bank=bank: e.activation(
                         self.oT[:, :, :],
                         bank[:, :].rearrange("p (c t) -> p c t", c=2), ACT.Copy))
            self.side_empty[k] = self.on("oT", key)
            yield
            bank, k = self.next_side()
            def project(e, bank=bank):
                for tt in range(2):
                    for c in range(2):
                        i = e.matmul(bank[:, tt * D:(tt + 1) * D], self.oT[:, c, tt * P:(tt + 1) * P],
                                     self.w_o[:, c, :], start=(c == 0), stop=(c == 1))
                return i
            self.put("pe", "out_proj", key, [self.side_empty[k], self.on("oT", key), self.weights], project)
            xs = net.x[:, b * T + 2 * pair:b * T + 2 * pair + 2, :]
            self.put("dve", "x_added", key, [self.on("out_proj", key), self.on("x_bias", b)],
                     lambda e, xs=xs, bank=bank: e.tensor_tensor(xs, bank[:, :].rearrange("p (t d) -> p t d", t=2), xs, ALU.add))
            self.side_empty[k] = self.on("x_added", key)
            yield
        row_stats(net, b, "output", self.on("x_added", (b, 1)))

    def run(self):
        pr, net = self.pr, self.net
        self.put("act", "table", 0, [], lambda e: e.preload_act_table_set("natural_log_exp_and_others"))
        self.set_ones()
        self.gathered = {}
        halves = 2 * net.B
        total = halves * HALF_UNITS
        side, split = Steps(), Steps()
        side.tasks += [self.prepare(0), self.prepare_values(0)]
        side.all()
        self.gather(0)
        if self.ratio:
            self.inverse_root(0)
        for n in range(total + BACK_LAG + len(ATTEND)):
            half, at = divmod(n, HALF_UNITS)
            if n % PAIR_UNITS == 0 and 0 < n <= total:
                split.tasks.append(self.split_maxima(n // PAIR_UNITS - 1))
                if n == total:
                    split.all()
            if n < total:
                if at == 0 and half + 1 < halves:
                    side.tasks.append(self.prepare(half + 1))
                if self.ratio and n + 1 < total:
                    self.inverse_root(n + 1)
                split.step()
                self.front(n, split)
                split.step()
            if at == VALUES_SLOT and half + 1 < halves:
                side.tasks.append(self.prepare_values(half + 1))
            if not self.ratio:
                side.step()
            back = n - BACK_LAG
            if 0 <= back < total:
                self.back(back)
            if n % PAIR_UNITS == TURN_SLOT and 0 < n // PAIR_UNITS <= total // PAIR_UNITS:
                self.turn_maxima(n // PAIR_UNITS - 1)
            if self.ratio:
                side.step()
            g, part = divmod(back - N_UNITS, N_UNITS)
            if g >= 0 and part < len(ATTEND) and g < total // N_UNITS:
                self.attend(g, part)
                if part == len(ATTEND) - 1:
                    self.evacuate(g)
                    side.tasks.append(self.finish_group(g))
            if at == GATHER_SLOT and half + 1 < halves:
                self.gather(half + 1)
        side.all()
        pr.run_block()


def attention(net, kind, weights):
    with ExitStack() as ctx:
        Attention(net, ctx, kind, weights).run()


F = 1024
FC = F // P
RANK = 64
DOWN_LAG = 2
H_BUFS = 4


class TernaryWeights:

    def __init__(self, net, ctx, args):
        self.net, self.args = net, args
        sb = lambda n, s: ctx.enter_context(net.nc.sbuf_tensor(f"ternary_{n}", s, F32))
        self.up = sb("w_up_T", [P, 2, F])
        self.down = sb("w_down_T", [P, FC, net.D])

    def make_scratch(self, ctx):
        sb = lambda n, s: ctx.enter_context(self.net.nc.sbuf_tensor(f"ternary_{n}", s, F32))
        self.loaded_w = sb("w_loaded", [P, 2, F * self.net.D // P])
        self.positive = sb("w_positive", [P, 2, F * self.net.D // P])
        self.negative = sb("w_negative", [P, 2, F * self.net.D // P])
        self.threshold = sb("w_threshold", [P, 2, 3])

    def load(self):
        for k, name in enumerate(("w_up", "w_down")):
            w = self.args[name]
            dst = self.loaded_w[:, k, :].rearrange("p (g n) -> p g n", g=w.shape[0] // P)
            self.net.program.put("sp", f"dma_{name}", 0, [], lambda e, dst=dst, w=w: e.dma_start(
                dst, w.rearrange("(g p) n -> p g n", p=P)))

    def steps(self, bank, empty):
        net, on, put = self.net, self.net.program.on, self.net.program.put
        both = [(k, self.loaded_w[:, k, :], self.positive[:, k, :], self.negative[:, k, :], self.threshold[:, k, :])
                for k in range(2)]
        for k, w, pos, neg, th in both:
            yield
            put("dve", "w_abs", k, [on("dma_w_down" if k else "dma_w_up", 0)],
                lambda e, w=w, pos=pos: e.scalar_tensor_tensor(
                    out=pos, in0=w, scalar=-1.0, in1=w, op0=ALU.mult, op1=ALU.max))
            yield
            put("dve", "w_abs_row", k, [on("w_abs", k)], lambda e, pos=pos, th=th: e.tensor_reduce(
                th[:, 0:1], pos, AX_X, ALU.add))
        for k, w, pos, neg, th in both:
            yield
            put("pe", "w_abs_sum", k, [on("w_abs_row", k), empty[0]], lambda e, th=th: e.matmul(
                bank[:, 0:1], net.ones, th[:, 0:1], start=True, stop=True))
            put("dve", "threshold", k, [on("w_abs_sum", k)], lambda e, th=th: e.tensor_scalar(
                th[:, 1:2], bank[:, 0:1], 1.0 / (F * net.D), 0.5, ALU.mult, ALU.mult))
            empty[0] = on("threshold", k)
            put("dve", "neg_threshold", k, [on("threshold", k)], lambda e, th=th: e.tensor_scalar(
                th[:, 2:3], th[:, 1:2], -1.0, None, ALU.mult))
            put("pool", "w_above", k, [on("threshold", k)], lambda e, w=w, pos=pos, th=th:
                e.tensor_scalar(pos, w, th[:, 1:2], None, ALU.is_gt))
            put("pool", "w_below", k, [on("neg_threshold", k)], lambda e, w=w, neg=neg, th=th:
                e.tensor_scalar(neg, w, th[:, 2:3], None, ALU.is_lt))
            for _ in range(2):
                yield
            put("pool", "w_t", k, [on("w_above", k), on("w_below", k)], lambda e, pos=pos, neg=neg:
                e.tensor_tensor(pos, pos, neg, ALU.subtract))
            yield
            put("pool", "w_t_less", k, [on("w_t", k)], lambda e, w=w, pos=pos: e.tensor_tensor(
                pos, pos, w, ALU.subtract))
            yield
            put("pool", "w_q", k, [on("w_t_less", k)], lambda e, w=w, pos=pos: e.tensor_tensor(
                pos, pos, w, ALU.add))
        for _ in range(3):
            yield
        for (k, w, pos, neg, th), name, dst in zip(both, ("w_up", "w_down"), (self.up, self.down)):
            n_r, n_c = self.args[name].shape[0] // P, self.args[name].shape[1] // P
            for at, (row, col) in enumerate((row, col) for col in range(n_c) for row in range(0, n_r, 2)):
                key = (k, at)
                def turn(e, row=row, col=col, pos=pos, cols=n_c * P):
                    for j in range(2):
                        i = e.transpose(bank[:, j * P:(j + 1) * P],
                                        pos[:, (row + j) * cols + col * P:(row + j) * cols + (col + 1) * P], net.ident)
                    return i
                put("pe", "w_turned", key, [on("w_q", k), empty[0]], turn)
                put("act", "w_ready", key, [on("w_turned", key)], lambda e, dst=dst, row=row, col=col: e.activation(
                    dst[:, col, row * P:(row + 2) * P], bank[:, 0:2 * P], ACT.Copy))
                self.ready = empty[0] = on("w_ready", key)
                yield


class FeedForward(Phase):

    def __init__(self, net, ctx, kind, args, ternary, result=None):
        super().__init__(net, kind)
        self.args, self.ternary, self.result = args, ternary, result
        self.low = kind == "lowrank"
        sb = lambda n, s, d=F32: ctx.enter_context(net.nc.sbuf_tensor(f"{kind}_{n}", s, d))
        L, D, T = net.L, net.D, net.T
        self.scale = sb("x_scale", [P, net.B * T])
        self.xn = sb("xn", [P, 2, D])
        self.xnT = sb("xn_T", [P, 2, 2, L])
        self.hidden = sb("hidden", [P, H_BUFS, L])
        if self.low:
            self.u1 = sb("u1", [P, 2, RANK])
            self.v1 = sb("v1", [RANK, F])
            self.u2 = sb("u2", [P, FC, RANK])
            self.v2 = sb("v2_twice", [P, D])
            self.b1 = sb("b1", [P, FC])
            self.b2 = sb("b2", [P, D])
            self.rank_in = sb("rank_in", [RANK, 2, L])
            self.rank_sums = sb("rank_out", [P, 2, L])
        else:
            self.rms = sb("x_rms", [P, net.B * T])
            self.up, self.down, self.weights = ternary.up, ternary.down, ternary.ready
            self.sq = sb("squares", [P, 2, L])
            self.sum = sb("square_sum", [P, 2, L])
            self.hs = sb("h_scale", [P, 2, T])
        bk = net.banks
        self.h_banks, self.down_banks = bk[0:2], bk[4:8]
        self.prep_bank, self.post_bank = bk[2], bk[3]
        self.prep_empty, self.post_empty = [None], None

    def load_weights(self):
        args = self.args
        n = [0]
        def load(dst, src, slow=False):
            self.put("sp", "dma_weights", n[0], [], lambda e: e.dma_start(
                dst, src, allow_slow_non_contiguous=True) if slow else e.dma_start(dst, src))
            n[0] += 1
        load(self.u1[:, :, :], args["U1"].rearrange("(c p) r -> p c r", p=P))
        load(self.v1[:, :], args["V1"])
        load(self.u2[:, :, :], args["U2"].rearrange("(f p) r -> p f r", p=P))
        for k in range(2):
            load(self.v2[k * RANK:(k + 1) * RANK, :], args["V2"])
        load(self.b1[:, :], args["b1"].rearrange("(f p) -> p f", p=P), slow=True)
        load(self.b2[:, :], args["b2"].partition_broadcast(P))
        self.weights = self.on("dma_weights", n[0] - 1)

    def scales(self):
        net = self.net
        var, scale = net.mean_var[:, :, 1], self.scale[:, :]
        self.put("act", "std", 0, [], lambda e: e.activation(scale, var, ACT.Sqrt, bias=net.eps_ln[:, :]))
        self.put("dve", "scale", 0, [self.on("std", 0)], lambda e: e.reciprocal(scale, scale))
        self.scaled = self.on("scale", 0)
        if self.low:
            return
        rms = self.rms[:, :]
        self.put("act", "std", 1, [], lambda e: e.activation(rms, var, ACT.Sqrt))
        self.put("dve", "rms", 0, [self.on("std", 1), self.on("scale", 0)],
                 lambda e: e.tensor_tensor(rms, rms, scale, ALU.mult))
        self.put("dve", "rms", 1, [self.on("rms", 0)], lambda e: e.tensor_scalar(rms, rms, 1e-8, None, ALU.add))
        self.put("dve", "rms", 2, [self.on("rms", 1)], lambda e: e.reciprocal(rms, rms))
        self.put("dve", "scale", 1, [self.on("rms", 2)], lambda e: e.tensor_tensor(scale, scale, rms, ALU.mult))
        self.scaled = self.on("scale", 1)

    def prepare(self, b):
        net, T, bank = self.net, self.net.T, self.prep_bank
        xb = b % 2
        in_use = self.on("rank_in", b - 2) if self.low else self.on("up", (b - 1) * FC - 1)
        for pair in range(T // 2):
            key = (b, pair)
            before = self.on("turned", (b, 0) if pair else (b - 1, T // 2 - 1))
            def normal(e, pair=pair):
                for tt in range(2):
                    t = b * T + 2 * pair + tt
                    i = e.tensor_scalar(self.xn[:, tt, :], net.x[:, t, :], net.mean_var[:, t, 0:1],
                                        self.scale[:, t:t + 1], ALU.subtract, ALU.mult)
                return i
            self.put("dve", "xn", key, [self.scaled, before], normal)
            yield
            self.put("pe", "turned", key, [self.on("xn", key), self.prep_empty[0]], lambda e, pair=pair: turn_blocks(
                e, bank, lambda t: self.xn[:, t % 2, :], pair, net.ident))
            self.put("dve", "xnT", key, [self.on("turned", key), in_use], lambda e, pair=pair: e.tensor_copy(
                self.xnT[:, xb, :, pair * 256:(pair + 1) * 256], bank[:, :].rearrange("p (c t) -> p c t", c=2)))
            self.prep_empty[0] = self.on("xnT", key)
        if not self.low:
            return
        yield
        def rank(e):
            for c in range(2):
                i = e.matmul(bank[0:RANK, :], self.u1[:, c, :], self.xnT[:, xb, c, :], start=(c == 0), stop=(c == 1))
            return i
        self.put("pe", "rank_in", b, [self.on("xnT", (b, 1)), self.prep_empty[0], self.weights], rank)
        self.put("dve", "rank_copy", b, [self.on("rank_in", b), self.on("up", (b - 1) * FC - 1)],
                 lambda e: e.tensor_copy(self.rank_in[:, xb, :], bank[0:RANK, :]))
        self.prep_empty[0] = self.on("rank_copy", b)
        self.put("pool", "x_bias", b, [self.on("xn", (b, 1)), self.weights], lambda e: e.tensor_tensor(
            net.xb(b), net.xb(b), self.b2[:, :].unsqueeze(1).to_broadcast([P, T, net.D]), ALU.add))

    def up_product(self, n):
        b, f = divmod(n, FC)
        bank, h = self.h_banks[n % 2], self.hidden[:, n % H_BUFS, :]
        def make(e):
            if self.low:
                return e.matmul(bank[:, :], self.v1[:, f * P:(f + 1) * P], self.rank_in[:, b % 2, :], start=True, stop=True)
            for c in range(2):
                i = e.matmul(bank[:, :], self.up[:, c, f * P:(f + 1) * P], self.xnT[:, b % 2, c, :],
                             start=(c == 0), stop=(c == 1))
            return i
        operand = self.on("rank_copy", b) if self.low else self.on("xnT", (b, 1))
        self.put("pe", "up", n, [operand, self.on("gelu", n - 2), self.weights], make)
        old = n - H_BUFS
        if self.low:
            self.put("act", "gelu", n, [self.on("up", n), self.weights, self.on("down", old | 1)],
                     lambda e: e.activation(h, bank[:, :], ACT.Gelu_apprx_tanh, bias=self.b1[:, f:f + 1]))
            return
        self.put("act", "gelu", n, [self.on("up", n), self.on("down", old), self.on("h_squared", old)],
                 lambda e: e.activation(h, bank[:, :], ACT.Gelu))
        total = self.sum[:, b % 2, :]
        if f == 0:
            self.put("dve", "h_squared", n, [self.on("gelu", n), self.on("h_rows", b - 2)],
                     lambda e: e.tensor_tensor(total, h, h, ALU.mult))
            return
        square = self.sq[:, n % 2, :]
        used = n - 4 if f == 2 else n - 2
        self.put("dve", "h_squared", n, [self.on("gelu", n), self.on("h_summed", used)],
                 lambda e: e.tensor_tensor(square, h, h, ALU.mult))
        before = self.on("h_squared", n - 1) if f == 1 else self.on("h_summed", n - 1)
        self.put("pool", "h_summed", n, [self.on("h_squared", n), before], lambda e: e.tensor_tensor(
            total, total, square, ALU.add))

    def down_product(self, n):
        T, D = self.net.T, self.net.D
        b, f = divmod(n, FC)
        if self.low:
            if f % 2 == 0:
                return
            bank = self.down_banks[b % 4]
            def make(e):
                for k in range(2):
                    i = e.matmul(bank[k * RANK:(k + 1) * RANK, :], self.u2[:, f - 1 + k, :],
                                 self.hidden[:, (n - 1 + k) % H_BUFS, :],
                                 start=(f == 1), stop=(f == FC - 1), skip_group_check=True)
                return i
            self.put("pe", "down", n, [self.on("gelu", n), self.on("rank_out", b - 4)], make)
            return
        banks = self.down_banks[2 * (b % 2):2 * (b % 2) + 2]
        def make(e):
            for t in range(T):
                i = e.matmul(banks[t // 2][:, (t % 2) * D:(t % 2 + 1) * D],
                             self.hidden[:, n % H_BUFS, t * P:(t + 1) * P], self.down[:, f, :],
                             start=(f == 0 and t % 2 == 0), stop=(f == FC - 1), skip_group_check=True)
            return i
        self.put("pe", "down", n, [self.on("gelu", n), self.on("x_added", (b - 2, 0)), self.weights], make)

    def complete(self, b):
        net, T, D, bank = self.net, self.net.T, self.net.D, self.post_bank
        done = self.on("down", (b + 1) * FC - 1)
        if self.low:
            self.put("dve", "rank_out", b, [done, self.on("ff_out", (b - 2, 1))],
                     lambda e: e.tensor_copy(self.rank_sums[:, b % 2, :], self.down_banks[b % 4][:, :]))
            yield
            for pair in range(T // 2):
                key = (b, pair)
                def make(e, pair=pair):
                    for tt in range(2):
                        t = 2 * pair + tt
                        i = e.matmul(bank[:, tt * D:(tt + 1) * D], self.rank_sums[:, b % 2, t * P:(t + 1) * P],
                                     self.v2[:, :], start=True, stop=True)
                    return i
                self.put("pe", "ff_out", key, [self.on("rank_out", b), self.post_empty, self.weights], make)
                yield
                xs = net.x[:, b * T + 2 * pair:b * T + 2 * pair + 2, :]
                self.put("dve", "x_added", key, [self.on("ff_out", key), self.on("x_bias", b)],
                         lambda e, xs=xs: e.tensor_tensor(xs, bank[:, :].rearrange("p (t d) -> p t d", t=2), xs, ALU.add))
                self.post_empty = self.on("x_added", key)
            return
        def row_sums(e):
            for t in range(T):
                i = e.matmul(bank[:, t:t + 1], self.sum[:, b % 2, t * P:(t + 1) * P], net.ones[:, 0:1],
                             start=True, stop=True)
            return i
        self.put("pe", "h_rows", b, [self.on("h_summed", (b + 1) * FC - 1), self.post_empty], row_sums)
        yield
        hs = self.hs[:, b % 2, :]
        self.put("act", "h_rms", b, [self.on("h_rows", b), self.on("x_added", (b - 2, 0))],
                 lambda e: e.activation(hs, bank[:, 0:T], ACT.Sqrt, scale=1.0 / F))
        self.post_empty = self.on("h_rms", b)
        self.put("dve", "h_rms_eps", b, [self.on("h_rms", b)], lambda e: e.tensor_scalar(hs, hs, 1e-8, None, ALU.add))
        self.put("dve", "h_scale", b, [self.on("h_rms_eps", b)], lambda e: e.reciprocal(hs, hs))
        def add(e):
            for t in range(T):
                xs = net.x[:, b * T + t, :]
                i = e.scalar_tensor_tensor(
                    out=xs, in0=self.down_banks[2 * (b % 2) + t // 2][:, (t % 2) * D:(t % 2 + 1) * D],
                    scalar=hs[:, t:t + 1], in1=xs, op0=ALU.mult, op1=ALU.add)
            return i
        self.put("dve", "x_added", (b, 0), [self.on("h_scale", b), done], add)
        self.put("sp", "dma_out", b, [self.on("x_added", (b, 0))], lambda e: e.dma_start(
            self.result[b].rearrange("(t p) d -> p t d", p=P), net.xb(b)))

    def run(self, next_weights):
        net = self.net
        prep, post, other = Steps(), Steps(), Steps()
        self.scales()
        if self.low:
            self.load_weights()
            self.ternary.load()
            next_weights.load()
            other.tasks.append(self.ternary.steps(self.prep_bank, self.prep_empty))
        prep.tasks.append(self.prepare(0))
        prep.all()
        n_slots = net.B * FC
        for n in range(n_slots + DOWN_LAG + 1):
            if n < n_slots:
                if n % FC == 0 and n // FC + 1 < net.B:
                    prep.tasks.append(self.prepare(n // FC + 1))
                self.up_product(n)
            m = n - DOWN_LAG
            if 0 <= m < n_slots:
                self.down_product(m)
            if m > 0 and m % FC == 0:
                post.tasks.append(self.complete(m // FC - 1))
            (prep if prep.tasks else other).step()
            post.step()
        post.all()
        other.all()
        if self.result is not None:
            self.put("sp", "end", 0, [self.pr.all_of("dma_out")], lambda e: e.nop())
        net.program.run_block()


def feed_forward(net, kind, args, ternary, next_weights=None, result=None):
    with ExitStack() as ctx:
        if kind == "lowrank":
            ternary.make_scratch(ctx)
        FeedForward(net, ctx, kind, args, ternary, result).run(next_weights)


def two_layer_kernel(nc, a, out):
    B, L, D = a["L0_attn_x"].shape
    with ExitStack() as ctx:
        net = Net(nc, ctx, B, L, D)
        with ExitStack() as first:
            ratio = AttentionWeights(net, first, "ratio", {
                "w_in": a["L0_attn_w_qkv"], "b_in": a["L0_attn_b_qkv"],
                "w_o": a["L0_attn_w_out"], "b_o": a["L0_attn_b_out"]})
            load_start(net, a["L0_attn_x"], a["const_f"], a["const_b"], ratio)
            attention(net, "ratio", ratio)
        ternary = TernaryWeights(net, ctx, {k: a[f"L1_ffn_{k}"] for k in ("w_up", "w_down")})
        zeroed = AttentionWeights(net, ctx, "zeroed", {
            "w_in": a["L1_attn_Wqkv"], "b_in": a["L1_attn_bqkv"],
            "w_o": a["L1_attn_Wr"], "b_o": a["L1_attn_br"]})
        feed_forward(net, "lowrank", {k: a[f"L0_ffn_{k}"] for k in ("U1", "V1", "b1", "U2", "V2", "b2")},
                     ternary, next_weights=zeroed)
        attention(net, "zeroed", zeroed)
        feed_forward(net, "ternary", None, ternary, result=out)


_INPUTS = ["L0_attn_x", "L0_attn_w_qkv", "L0_attn_b_qkv", "L0_attn_w_out", "L0_attn_b_out", "L0_ffn_U1",
           "L0_ffn_V1", "L0_ffn_b1", "L0_ffn_U2", "L0_ffn_V2", "L0_ffn_b2", "L1_attn_Wqkv", "L1_attn_bqkv",
           "L1_attn_Wr", "L1_attn_br", "L1_ffn_w_up", "L1_ffn_w_down"]


def kernel(**inputs):
    import concourse.bacc as _bacc
    from concourse.bass_utils import run_bass_kernel_spmd as _run

    nc = _bacc.Bacc("TRN2", target_bir_lowering=False, num_devices=1)
    const_f, const_b = constants()
    arrays = {name: np.ascontiguousarray(inputs[name]) for name in _INPUTS}
    arrays |= {"const_f": const_f, "const_b": const_b}
    aps = {name: nc.dram_tensor(f"in_{name}", a.shape, mybir.dt.from_np(a.dtype), kind="ExternalInput").ap()
           for name, a in arrays.items()}
    shape = arrays["L0_attn_x"].shape
    out = nc.dram_tensor("out", shape, F32, kind="ExternalOutput").ap()
    two_layer_kernel(nc, aps, out)
    r = _run(nc, [{f"in_{name}": a for name, a in arrays.items()}], core_ids=[0])
    return r.results[0]["out"]
```
